# Optimizing a Trainium2 kernel written in Bass

```python
import numpy as np
import jax
import jax.numpy as jnp

def _softmax(x, axis=-1):
    return jax.nn.softmax(x, axis=axis)

def _gelu(x):
    return jax.nn.gelu(x, approximate=True)

def _silu(x):
    return jax.nn.silu(x)

def _sigmoid(x):
    return jax.nn.sigmoid(x)

def _layernorm(x, axis=-1, eps=1e-05):
    m = jnp.mean(x, axis=axis, keepdims=True)
    v = jnp.var(x, axis=axis, keepdims=True)
    return (x - m) / jnp.sqrt(v + eps)

def _scatter_add(tgt, idx, src, axis=0):
    return tgt.at[idx].add(src)

def _segment_sum(src, seg, n):
    return jax.ops.segment_sum(src, seg, n)
kernel_name = 'mk_rec_standalone_d1_rec_r8_b4fa67'

def setup_inputs(seed: int=0):
    np.random.seed(seed)
    _w = jnp.asarray

    def _rec_inputs():
        import jax
        import jax.numpy as jnp
        _rk = jax.random.key(seed)
        r_x = -9.29491e-05 + 1.00016 * jax.random.normal(jax.random.fold_in(_rk, 1), (2048, 39, 64), jnp.float32)
        return r_x
    r_x = _rec_inputs()

    def _L0_rec_setup():
        import jax, jax.numpy as jnp
        import numpy as np
        key = jax.random.key(seed)
        ks = jax.random.split(key, 4)
        B, F, D, A = (256, 39, 64, 64)
        x = jax.random.normal(ks[0], (B, F, D), dtype=jnp.float32)
        W_w = jax.random.normal(ks[1], (D, A), dtype=jnp.float32) * (1.0 / np.sqrt(D))
        b_w = jnp.zeros((A,), dtype=jnp.float32)
        W_h = jax.random.normal(ks[2], (A,), dtype=jnp.float32) * (1.0 / np.sqrt(A))
        b_h = jnp.zeros((1,), dtype=jnp.float32)
        W_p = jax.random.normal(ks[3], (D, 1), dtype=jnp.float32) * (1.0 / np.sqrt(D))
        b_p = jnp.zeros((1,), dtype=jnp.float32)
        return {'x': x, 'W_w': W_w, 'b_w': b_w, 'W_h': W_h, 'b_h': b_h, 'W_p': W_p, 'b_p': b_p}
    _L0_rec_all = _L0_rec_setup()
    _L0_rec_in = {k: v for k, v in _L0_rec_all.items() if k in ('W_w', 'b_w', 'W_h', 'b_h', 'W_p', 'b_p')}
    del _L0_rec_all
    return {'r_x': r_x, 'L0_rec_W_w': _L0_rec_in['W_w'], 'L0_rec_b_w': _L0_rec_in['b_w'], 'L0_rec_W_h': _L0_rec_in['W_h'], 'L0_rec_b_h': _L0_rec_in['b_h'], 'L0_rec_W_p': _L0_rec_in['W_p'], 'L0_rec_b_p': _L0_rec_in['b_p']}

def reference(r_x, L0_rec_W_w, L0_rec_b_w, L0_rec_W_h, L0_rec_b_h, L0_rec_W_p, L0_rec_b_p):
    import jax
    import jax.numpy as jnp

    def _L0_rec_ref(x, W_w, b_w, W_h, b_h, W_p, b_p):
        import jax, jax.numpy as jnp
        import numpy as np
        B, F, D = x.shape
        row, col = np.triu_indices(F, k=1)
        ip = x[:, row, :] * x[:, col, :]
        hidden = jax.nn.relu(jnp.einsum('bpd,da->bpa', ip, W_w) + b_w)
        logits = jnp.einsum('bpa,a->bp', hidden, W_h) + b_h[0]
        a = jax.nn.softmax(logits, axis=1)[:, :, None]
        pooled = jnp.sum(a * ip, axis=1)
        return pooled @ W_p + b_p
    y = _L0_rec_ref(r_x, L0_rec_W_w, L0_rec_b_w, L0_rec_W_h, L0_rec_b_h, L0_rec_W_p, L0_rec_b_p)
    return y

_drawn_inputs = setup_inputs


def setup_inputs(seed=0):
    import zlib

    import numpy as np

    out = dict(_drawn_inputs(seed))
    spreads = {'L0_rec_b_w': (0.0, 0.1)}
    factors = {}
    for name, (base, spread) in spreads.items():
        noise = np.random.default_rng([zlib.crc32(name.encode()), seed]).standard_normal(out[name].shape)
        drawn = base * np.exp(spread * noise) if base else spread * noise
        out[name] = jnp.asarray(drawn.astype(out[name].dtype))
    for name, factor in factors.items():
        out[name] = (out[name] * factor).astype(out[name].dtype)
    return out
```

```python
import concourse.bass as bass
from concourse import mybir
from contextlib import ExitStack


def bass_pairwise_attention_pooling(
    nc: bass.Bass,
    x: bass.AP,
    w_hidden: bass.AP,
    b_hidden: bass.AP,
    w_logit: bass.AP,
    b_logit: bass.AP,
    w_out: bass.AP,
    b_out: bass.AP,
    y: bass.AP,
):
    fp32 = mybir.dt.float32
    bf16 = mybir.dt.bfloat16
    ALU = mybir.AluOpType
    ACT = mybir.ActivationFunctionType
    AX = mybir.AxisListType

    BATCHES, FIELDS, D = x.shape
    A = w_hidden.shape[1]
    P = 2 * D
    assert P == 128 and A == D and FIELDS % 2 == 1
    HALF = BATCHES // 2
    OFFSETS = FIELDS // 2
    PAIRS = FIELDS * OFFSETS
    WIDE = FIELDS + OFFSETS

    QUADS = 4
    BODY = 4
    GROUP_STEPS = P // 2 // QUADS
    GROUP_BODIES = GROUP_STEPS // BODY
    GROUPS = HALF // (GROUP_STEPS * QUADS)
    BODIES = GROUPS * GROUP_BODIES

    UNIT_DUOS = 2 * QUADS
    UNITS = HALF // UNIT_DUOS
    CHUNKS = UNIT_DUOS // 2
    ROWS = 2 * FIELDS

    BANK = 512
    ZCOLS = (PAIRS + 1) // 2
    HCOLS = PAIRS // 3
    assert 3 * HCOLS == PAIRS and HCOLS <= BANK // 2

    x_rows_dram = x.rearrange("(h c r) f d -> h (r f) c d", h=2, r=2)
    y_dram = y.rearrange("(h g t q) o -> q h t (g o)", h=2, g=GROUPS, q=QUADS)

    ctx = ExitStack()
    with ctx:
        def sb(name, shape, dt=fp32):
            return ctx.enter_context(nc.sbuf_tensor(name, shape, dt))

        def ps(name, shape):
            return ctx.enter_context(nc.psum_tensor(name, shape, fp32))

        def sem(name):
            return ctx.enter_context(nc.semaphore(name))

        w_block = sb("w_block", [P, P])
        b_col = sb("b_col", [P, 1])
        head_cols = sb("head_cols", [P, 2, 47])
        head_w = sb("head_w", [P, 2, BODY, 32])
        bh_col = sb("bh_col", [P, 1])
        bp_col = sb("bp_col", [P, 1])
        ident = sb("ident", [ROWS, ROWS])
        zero_row = sb("zero_row", [1, BANK], bf16)
        x_rows = sb("x_rows", [ROWS, 2, CHUNKS, 2 * D])
        x_wide = sb("x_wide", [P, 2, UNIT_DUOS, WIDE])
        prod = sb("prod", [P, BODY, QUADS, 2 * ZCOLS])
        hidden = sb("hidden", [P, 2, QUADS, 2 * ZCOLS])
        neg_max = sb("neg_max", [P, 1])
        exp_bias = sb("exp_bias", [P, 1])
        exps = sb("exps", [P, 3, HCOLS])
        weighted = sb("weighted", [P, 3, HCOLS])
        exp_sum = sb("exp_sum", [P, 1])
        pooled = sb("pooled", [P, 1])
        inv_sum = sb("inv_sum", [P, 1])
        y_all = sb("y_all", [P, GROUPS])

        z = ps("z", [P, 2, 2, BANK])
        heads = ps("heads", [P, 6, BANK // 2])
        x_cols = ps("x_cols", [P, BANK])
        logits = heads[:, 0:3, 0:HCOLS]
        values = heads[:, 3:6, 0:HCOLS]

        zeroed = sem("zeroed")
        params = sem("params")
        ident_ready = sem("ident_ready")
        x_loaded = [sem("x_loaded0"), sem("x_loaded1")]
        x_transposed = sem("x_transposed")
        x_spread = sem("x_spread")
        prod_ready = sem("prod_ready")
        z_ready = sem("z_ready")
        hidden_ready = sem("hidden_ready")
        head_w_ready = sem("head_w_ready")
        heads_done = sem("heads_done")
        max_ready = sem("max_ready")
        bias_ready = sem("bias_ready")
        exps_ready = sem("exps_ready")
        pooled_ready = sem("pooled_ready")
        inv_ready = sem("inv_ready")
        y_ready = sem("y_ready")
        y_stored = sem("y_stored")

        N_PARAMS = 10

        block = ctx.enter_context(nc.Block())

        @block.sync
        def _(sp):
            def load(unit, slot):
                for h in range(2):
                    sp.dma_start(x_rows[:, slot, :, h * D:(h + 1) * D],
                                 x_rows_dram[h, :, bass.ds(unit * CHUNKS, CHUNKS), :]).then_inc(x_loaded[slot], 16)

            load(0, 0)
            load(1, 1)
            sp.wait_ge(zeroed, 1)
            for h in range(2):
                rows = slice(h * D, (h + 1) * D)
                at = 15 + 16 * h
                sp.dma_start(w_block[rows, rows], w_hidden).then_inc(params, 16)
                sp.dma_start(b_col[rows, :], b_hidden.rearrange("(a o) -> a o", o=1)).then_inc(params, 16)
                sp.dma_start(head_cols[rows, 0, at:at + 1],
                             w_logit.rearrange("(a o) -> a o", o=1)).then_inc(params, 16)
                sp.dma_start(head_cols[rows, 1, at:at + 1], w_out).then_inc(params, 16)
            sp.dma_start(bh_col[:, :], b_logit.rearrange("(a o) -> a o", o=1).broadcast_to((P, 1))).then_inc(params, 16)
            sp.dma_start(bp_col[:, :], b_out.rearrange("(a o) -> a o", o=1).broadcast_to((P, 1))).then_inc(params, 16)

            with sp.Fori(1, UNITS // 2) as u:
                for slot in range(2):
                    sp.wait_ge(x_transposed, 2 * u + slot - 1)
                    load(2 * u + slot, slot)

            sp.wait_ge(y_ready, GROUPS)
            for q in range(QUADS):
                for h in range(2):
                    at = 32 * q + 16 * h
                    sp.dma_start(y_dram[q, h, :, :], y_all[at:at + GROUP_STEPS, :],
                                 allow_slow_non_contiguous=True).then_inc(y_stored, 16)
            sp.wait_ge(y_stored, 16 * 2 * QUADS)

        @block.gpsimd
        def _(pool):
            nc.gpsimd.memset(ident[:, :], 0.0).then_inc(ident_ready, 1)
            pool.wait_ge(ident_ready, 1)
            nc.gpsimd.affine_select(out=ident[:, :], in_=ident[:, :], compare_op=ALU.not_equal, fill=1.0,
                                    base=0, pattern=[[-1, ROWS]], channel_multiplier=1).then_inc(ident_ready, 1)

        @block.vector
        def _(dve):
            nc.vector.memset(w_block[:, :], 0.0)
            nc.vector.memset(zero_row[:, :], 0.0)
            nc.vector.memset(prod[:, :, :, PAIRS:2 * ZCOLS], 0.0)
            nc.vector.memset(head_cols[:, :, :], 0.0).then_inc(zeroed, 1)

            def multiply(step, e):
                slot, duo = e // 2, QUADS * (e % 2)
                x0 = x_wide[:, slot, duo:duo + QUADS, 0:FIELDS]
                one = bass.AP(x0.tensor, x0.offset, [x0.ap[0], x0.ap[1], [0, OFFSETS], x0.ap[2]])
                x1 = x_wide[:, slot, duo:duo + QUADS, 1:1 + FIELDS]
                other = bass.AP(x1.tensor, x1.offset, [x1.ap[0], x1.ap[1], [1, OFFSETS], x1.ap[2]])
                dve.wait_ge(x_spread, step - e + 2 * (e // 2) + 2)
                if not (isinstance(step, int) and step < BODY):
                    dve.wait_ge(heads_done, step - BODY + 1)
                nc.vector.tensor_tensor(
                    prod[:, e, :, 0:PAIRS].rearrange("p q (k i) -> p q k i", k=OFFSETS), one, other,
                    ALU.mult).then_inc(prod_ready, 1)

            def pool_group(g):
                dve.wait_ge(heads_done, GROUP_STEPS * (g + 1))
                nc.vector.tensor_reduce(neg_max[:, :], logits, AX.XY, ALU.max, negate=True).then_inc(max_ready, 1)
                dve.wait_ge(max_ready, g + 1)
                nc.vector.tensor_scalar(exp_bias[:, :], neg_max[:, :], bh_col[:, 0:1], bh_col[:, 0:1],
                                        ALU.subtract, ALU.add).then_inc(bias_ready, 1)
                dve.wait_ge(exps_ready, g + 1)
                nc.vector.tensor_tensor_reduce(out=weighted[:, :, :], in0=exps[:, :, :], in1=values, scale=1.0,
                                               scalar=0.0, op0=ALU.mult, op1=ALU.add,
                                               accum_out=pooled[:, :]).then_inc(pooled_ready, 1)
                nc.vector.reciprocal(inv_sum[:, :], exp_sum[:, :]).then_inc(inv_ready, 1)
                dve.wait_ge(pooled_ready, g + 1)
                dve.wait_ge(inv_ready, g + 1)
                nc.vector.tensor_scalar(y_all[:, bass.ds(g, 1)], pooled[:, :], inv_sum[:, 0:1], bp_col[:, 0:1],
                                        ALU.mult, ALU.add).then_inc(y_ready, 1)

            LEAD = 2

            def ahead(step0, steps=BODY):
                for e in range(steps):
                    multiply(step0 + LEAD + e, (LEAD + e) % BODY)

            for e in range(LEAD):
                multiply(e, e)
            ahead(0)
            with dve.Fori(1, GROUP_BODIES) as w:
                ahead(BODY * w)
            dve.wait_ge(params, 16 * N_PARAMS)
            pool_group(0)
            with dve.Fori(1, GROUPS - 1) as g:
                with dve.Fori(0, GROUP_BODIES) as w:
                    ahead(GROUP_STEPS * g + BODY * w)
                pool_group(g)
            with dve.Fori(BODIES - GROUP_BODIES, BODIES - 1) as v:
                ahead(BODY * v)
            ahead(BODY * (BODIES - 1), BODY - LEAD)
            pool_group(GROUPS - 1)

        @block.scalar
        def _(act):
            def spread(unit, slot):
                cols = x_cols[:, 0:UNIT_DUOS * FIELDS].rearrange("p (u f) -> p u f", f=FIELDS)
                act.wait_ge(x_transposed, unit + 1)
                if not (isinstance(unit, int) and unit < 2):
                    act.wait_ge(prod_ready, 2 * unit - 2)
                nc.scalar.copy(x_wide[:, slot, :, 0:FIELDS], cols).then_inc(x_spread, 1)
                nc.scalar.copy(x_wide[:, slot, :, FIELDS:WIDE], cols[:, :, 0:OFFSETS]).then_inc(x_spread, 1)

            def place_heads(w):
                first = head_cols[:, :, bass.ds(15 - (BODY - 1) - BODY * w, 32)]
                windows = bass.AP(first.tensor, first.offset, [first.ap[0], first.ap[1], [1, BODY], [1, 32]])
                nc.scalar.copy(head_w[:, :, :, :], windows).then_inc(head_w_ready, 1)

            def rectify(step, parity, w=None):
                if not (isinstance(step, int) and step < 2):
                    act.wait_ge(heads_done, step - 1)
                for q in range(QUADS):
                    act.wait_ge(z_ready, QUADS * step + q + 1)
                    nc.scalar.activation(hidden[:, parity, q, :].rearrange("p (b n) -> p b n", b=2),
                                         z[:, q % 2, :, 0:ZCOLS], ACT.Relu,
                                         bias=b_col[:, 0:1]).then_inc(hidden_ready, 1)
                    if w is not None and q == 1:
                        place_heads(w)

            def exponentials(g):
                act.wait_ge(bias_ready, g + 1)
                nc.scalar.activation(exps[:, :, :], logits, ACT.Exp, bias=exp_bias[:, 0:1],
                                     accum_out=exp_sum[:, :]).then_inc(exps_ready, 1)

            def body(group, w, last=False):
                v = GROUP_BODIES * group + w
                for e in range(BODY):
                    if not (last and e == BODY - 1):
                        rectify(BODY * v + e + 1, (e + 1) % 2, w if e == 0 else None)
                    if e % 2 == 1 and not (isinstance(v, int) and 2 * v + 3 + e // 2 >= UNITS):
                        spread(2 * v + 3 + e // 2, (1 + e // 2) % 2)

            for unit in range(3):
                spread(unit, unit % 2)
            act.wait_ge(params, 16 * N_PARAMS)
            rectify(0, 0)
            body(0, 0)
            with act.Fori(1, GROUP_BODIES) as w:
                body(0, w)
            exponentials(0)
            with act.Fori(1, GROUPS - 1) as g:
                with act.Fori(0, GROUP_BODIES) as w:
                    body(g, w)
                exponentials(g)
            with act.Fori(0, GROUP_BODIES - 2) as w:
                body(GROUPS - 1, w)
            body(GROUPS - 1, GROUP_BODIES - 2)
            body(GROUPS - 1, GROUP_BODIES - 1, last=True)
            exponentials(GROUPS - 1)

        @block.tensor
        def _(pe):
            def transpose_unit(unit, slot, loads):
                pe.wait_ge(x_loaded[slot], 32 * loads)
                if not (isinstance(unit, int) and unit == 0):
                    pe.wait_ge(x_spread, 2 * unit)
                for c in range(CHUNKS):
                    last = nc.tensor.transpose(x_cols[:, c * ROWS:(c + 1) * ROWS], x_rows[:, slot, c, :], ident[:, :])
                last.then_inc(x_transposed, 1)

            def hidden_layer(step, e):
                pe.wait_ge(prod_ready, step + 1)
                for q in range(QUADS):
                    if not (isinstance(step, int) and QUADS * step + q < 2):
                        pe.wait_ge(hidden_ready, QUADS * step + q - 1)
                    for b in range(2):
                        last = nc.tensor.matmul(z[:, q % 2, b, 0:ZCOLS], w_block[:, :],
                                                prod[:, e, q, b * ZCOLS:(b + 1) * ZCOLS], start=True, stop=True)
                    last.then_inc(z_ready, 1)

            def open_group(g):
                if not (isinstance(g, int) and g == 0):
                    pe.wait_ge(pooled_ready, g)
                for b in range(3):
                    nc.tensor.matmul(heads[:, 2 * b:2 * b + 2, :], zero_row[:, 0:P], zero_row[:, :],
                                     start=True, stop=False, skip_group_check=True)

            def two_heads(step, e):
                pe.wait_ge(hidden_ready, QUADS * (step + 1))
                for kind, source in ((0, hidden[:, e % 2, :, :]), (1, prod[:, e, :, :])):
                    for c in range(3):
                        for q in range(QUADS):
                            last = nc.tensor.matmul(heads[32 * q:32 * q + 32, 3 * kind + c, 0:HCOLS],
                                                    head_w[:, kind, BODY - 1 - e, :],
                                                    source[:, q, c * HCOLS:(c + 1) * HCOLS],
                                                    start=False, stop=True, skip_group_check=True,
                                                    tile_position=(0, 32 * q))
                last.then_inc(heads_done, 1)

            def body(v, opens=None, last=False):
                for e in range(BODY):
                    step = BODY * v + e
                    if not (last and e == BODY - 1):
                        hidden_layer(step + 1, (e + 1) % BODY)
                    if e % 2 == 1:
                        unit = 2 * v + 3 + e // 2
                        if not (isinstance(v, int) and unit >= UNITS):
                            transpose_unit(unit, (1 + e // 2) % 2, v + 2 + e // 2)
                    if e == 0:
                        pe.wait_ge(head_w_ready, v + 1)
                        if opens is not None:
                            open_group(opens)
                    two_heads(step, e)

            pe.wait_ge(ident_ready, 2)
            for unit in range(3):
                transpose_unit(unit, unit % 2, unit // 2 + 1)
            pe.wait_ge(params, 16 * N_PARAMS)
            hidden_layer(0, 0)
            body(0, opens=0)
            with pe.Fori(1, GROUP_BODIES) as v:
                body(v)
            with pe.Fori(1, GROUPS - 1) as g:
                body(GROUP_BODIES * g, opens=g)
                with pe.Fori(1, GROUP_BODIES) as w:
                    body(GROUP_BODIES * g + w)
            body(BODIES - GROUP_BODIES, opens=GROUPS - 1)
            with pe.Fori(BODIES - GROUP_BODIES + 1, BODIES - 2) as v:
                body(v)
            body(BODIES - 2)
            body(BODIES - 1, last=True)


_INS = ['r_x', 'L0_rec_W_w', 'L0_rec_b_w', 'L0_rec_W_h', 'L0_rec_b_h', 'L0_rec_W_p', 'L0_rec_b_p']
_OUTS = [((2048, 1), 'float32')]


def kernel(**inputs):
    import numpy as _np
    import concourse.bacc as _bacc
    from concourse import mybir as _mybir
    from concourse.bass_utils import run_bass_kernel_spmd as _run

    nc = _bacc.Bacc("TRN2", target_bir_lowering=False, num_devices=1)
    arrays, args = {}, []
    for name in _INS:
        a = _np.ascontiguousarray(inputs[name])
        arrays[f"in_{name}_dram"] = a
        args.append(nc.dram_tensor(f"in_{name}_dram", a.shape, _mybir.dt.from_np(a.dtype), kind="ExternalInput").ap())
    for i, (shape, dtype) in enumerate(_OUTS):
        dt = _mybir.dt.from_np(_np.dtype(dtype))
        args.append(nc.dram_tensor(f"out_{i}_dram", shape, dt, kind="ExternalOutput").ap())
    bass_pairwise_attention_pooling(nc, *args)
    r = _run(nc, [arrays], core_ids=[0])
    return r.results[0]["out_0_dram"]
```

```python
import concourse.bass as bass
from concourse import mybir
from contextlib import ExitStack


def bass_pairwise_attention_pooling(
    nc: bass.Bass,
    x: bass.AP,
    w_hidden: bass.AP,
    b_hidden: bass.AP,
    w_logit: bass.AP,
    b_logit: bass.AP,
    w_out: bass.AP,
    b_out: bass.AP,
    y: bass.AP,
):
    fp32r = mybir.dt.float32r
    fp32 = mybir.dt.float32
    bf16 = mybir.dt.bfloat16
    ALU = mybir.AluOpType
    ACT = mybir.ActivationFunctionType
    AX = mybir.AxisListType

    BATCHES, FIELDS, D = x.shape
    A = w_hidden.shape[1]
    P = 2 * D
    assert P == 128 and A == D and FIELDS % 2 == 1
    HALF = BATCHES // 2
    OFFSETS = FIELDS // 2
    PAIRS = FIELDS * OFFSETS
    WIDE = FIELDS + OFFSETS

    QUADS = 4
    SPLIT = 3
    BODY = 4
    GROUP_STEPS = P // 2 // QUADS
    GROUP_BODIES = GROUP_STEPS // BODY
    GROUPS = HALF // (GROUP_STEPS * QUADS)
    BODIES = GROUPS * GROUP_BODIES

    UNIT_DUOS = 2 * QUADS
    UNITS = HALF // UNIT_DUOS
    CHUNKS = UNIT_DUOS // 2
    ROWS = 2 * FIELDS

    BANK = 512
    ZCOLS = (PAIRS + 3) // 4 * 2
    HCOLS = PAIRS // 3
    assert 3 * HCOLS == PAIRS and HCOLS <= BANK // 2

    x_rows_dram = x.rearrange("(h c r) f d -> h (r f) c d", h=2, r=2)
    y_dram = y.rearrange("(h g t q) o -> q h t (g o)", h=2, g=GROUPS, q=QUADS)

    ctx = ExitStack()
    with ctx:
        def sb(name, shape, dt=fp32):
            return ctx.enter_context(nc.sbuf_tensor(name, shape, dt))

        def ps(name, shape):
            return ctx.enter_context(nc.psum_tensor(name, shape, fp32))

        def sem(name):
            return ctx.enter_context(nc.semaphore(name))

        w_block = sb("w_block", [P, P])
        w_high = sb("w_high", [P, P], fp32r)
        w_low = sb("w_low", [P, P], fp32r)
        b_col = sb("b_col", [P, 1])
        head_cols = sb("head_cols", [P, 2, 47])
        head_w = sb("head_w", [P, 2, BODY, 32])
        bh_col = sb("bh_col", [P, 1])
        bp_col = sb("bp_col", [P, 1])
        ident = sb("ident", [ROWS, ROWS])
        zero_row = sb("zero_row", [1, BANK], bf16)
        x_rows = sb("x_rows", [ROWS, 2, CHUNKS, 2 * D])
        x_wide = sb("x_wide", [P, 2, UNIT_DUOS, WIDE])
        prod = sb("prod", [P, BODY, QUADS, 2 * ZCOLS])
        high = sb("high", [P, BODY, SPLIT, 2 * ZCOLS], fp32r)
        low = sb("low", [P, BODY, SPLIT, 2 * ZCOLS], fp32r)
        hidden = sb("hidden", [P, 2, QUADS, 2 * ZCOLS])
        neg_max = sb("neg_max", [P, 1])
        exp_bias = sb("exp_bias", [P, 1])
        exps = sb("exps", [P, 3, HCOLS])
        weighted = sb("weighted", [P, 3, HCOLS])
        exp_sum = sb("exp_sum", [P, 1])
        pooled = sb("pooled", [P, 1])
        inv_sum = sb("inv_sum", [P, 1])
        y_all = sb("y_all", [P, GROUPS])

        z = ps("z", [P, 2, 2, BANK])
        heads = ps("heads", [P, 6, BANK // 2])
        x_cols = ps("x_cols", [P, BANK])
        logits = heads[:, 0:3, 0:HCOLS]
        values = heads[:, 3:6, 0:HCOLS]

        zeroed = sem("zeroed")
        params = sem("params")
        ident_ready = sem("ident_ready")
        x_loaded = [sem("x_loaded0"), sem("x_loaded1")]
        x_transposed = sem("x_transposed")
        x_spread = sem("x_spread")
        prod_ready = sem("prod_ready")
        w_high_ready = sem("w_high_ready")
        w_low_ready = sem("w_low_ready")
        high_ready = sem("high_ready")
        low_ready = sem("low_ready")
        z_ready = sem("z_ready")
        hidden_ready = sem("hidden_ready")
        head_w_ready = sem("head_w_ready")
        values_done = sem("values_done")
        logits_done = sem("logits_done")
        max_ready = sem("max_ready")
        bias_ready = sem("bias_ready")
        exps_ready = sem("exps_ready")
        pooled_ready = sem("pooled_ready")
        inv_ready = sem("inv_ready")
        y_ready = sem("y_ready")
        y_stored = sem("y_stored")

        N_PARAMS = 10

        block = ctx.enter_context(nc.Block())

        @block.sync
        def _(sp):
            def load(unit, slot):
                for h in range(2):
                    sp.dma_start(x_rows[:, slot, :, h * D:(h + 1) * D],
                                 x_rows_dram[h, :, bass.ds(unit * CHUNKS, CHUNKS), :]).then_inc(x_loaded[slot], 16)

            load(0, 0)
            load(1, 1)
            sp.wait_ge(zeroed, 1)
            for h in range(2):
                rows = slice(h * D, (h + 1) * D)
                at = 15 + 16 * h
                sp.dma_start(w_block[rows, rows], w_hidden).then_inc(params, 16)
                sp.dma_start(b_col[rows, :], b_hidden.rearrange("(a o) -> a o", o=1)).then_inc(params, 16)
                sp.dma_start(head_cols[rows, 0, at:at + 1],
                             w_logit.rearrange("(a o) -> a o", o=1)).then_inc(params, 16)
                sp.dma_start(head_cols[rows, 1, at:at + 1], w_out).then_inc(params, 16)
            sp.dma_start(bh_col[:, :], b_logit.rearrange("(a o) -> a o", o=1).broadcast_to((P, 1))).then_inc(params, 16)
            sp.dma_start(bp_col[:, :], b_out.rearrange("(a o) -> a o", o=1).broadcast_to((P, 1))).then_inc(params, 16)

            with sp.Fori(1, UNITS // 2) as u:
                for slot in range(2):
                    sp.wait_ge(x_transposed, 2 * u + slot - 1)
                    load(2 * u + slot, slot)

            sp.wait_ge(y_ready, GROUPS)
            for q in range(QUADS):
                for h in range(2):
                    at = 32 * q + 16 * h
                    sp.dma_start(y_dram[q, h, :, :], y_all[at:at + GROUP_STEPS, :],
                                 allow_slow_non_contiguous=True).then_inc(y_stored, 16)
            sp.wait_ge(y_stored, 16 * 2 * QUADS)

        @block.gpsimd
        def _(pool):
            nc.gpsimd.memset(ident[:, :], 0.0).then_inc(ident_ready, 1)
            pool.wait_ge(ident_ready, 1)
            nc.gpsimd.affine_select(out=ident[:, :], in_=ident[:, :], compare_op=ALU.not_equal, fill=1.0,
                                    base=0, pattern=[[-1, ROWS]], channel_multiplier=1).then_inc(ident_ready, 1)

        @block.vector
        def _(dve):
            nc.vector.memset(w_block[:, :], 0.0)
            nc.vector.memset(zero_row[:, :], 0.0)
            nc.vector.memset(prod[:, :, :, PAIRS:2 * ZCOLS], 0.0)
            nc.vector.memset(head_cols[:, :, :], 0.0).then_inc(zeroed, 1)

            def multiply(step, e):
                slot, duo = e // 2, QUADS * (e % 2)
                x0 = x_wide[:, slot, duo:duo + QUADS, 0:FIELDS]
                one = bass.AP(x0.tensor, x0.offset, [x0.ap[0], x0.ap[1], [0, OFFSETS], x0.ap[2]])
                x1 = x_wide[:, slot, duo:duo + QUADS, 1:1 + FIELDS]
                other = bass.AP(x1.tensor, x1.offset, [x1.ap[0], x1.ap[1], [1, OFFSETS], x1.ap[2]])
                dve.wait_ge(x_spread, step - e + 2 * (e // 2) + 2)
                if not (isinstance(step, int) and step < BODY):
                    dve.wait_ge(values_done, step - BODY + 1)
                nc.vector.tensor_tensor(
                    prod[:, e, :, 0:PAIRS].rearrange("p q (k i) -> p q k i", k=OFFSETS), one, other,
                    ALU.mult).then_inc(prod_ready, 1)

            def residual(step, e):
                dve.wait_ge(high_ready, SPLIT * (step + 1))
                nc.vector.tensor_tensor(low[:, e, :, :], prod[:, e, 0:SPLIT, :], high[:, e, :, :].bitcast(fp32),
                                        ALU.subtract).then_inc(low_ready, 1)

            def pool_group(g):
                dve.wait_ge(values_done, GROUP_STEPS * (g + 1))
                dve.wait_ge(logits_done, GROUP_STEPS * (g + 1))
                nc.vector.tensor_reduce(neg_max[:, :], logits, AX.XY, ALU.max, negate=True).then_inc(max_ready, 1)
                dve.wait_ge(max_ready, g + 1)
                nc.vector.tensor_scalar(exp_bias[:, :], neg_max[:, :], bh_col[:, 0:1], bh_col[:, 0:1],
                                        ALU.subtract, ALU.add).then_inc(bias_ready, 1)
                dve.wait_ge(exps_ready, g + 1)
                nc.vector.tensor_tensor_reduce(out=weighted[:, :, :], in0=exps[:, :, :], in1=values, scale=1.0,
                                               scalar=0.0, op0=ALU.mult, op1=ALU.add,
                                               accum_out=pooled[:, :]).then_inc(pooled_ready, 1)
                nc.vector.reciprocal(inv_sum[:, :], exp_sum[:, :]).then_inc(inv_ready, 1)
                dve.wait_ge(pooled_ready, g + 1)
                dve.wait_ge(inv_ready, g + 1)
                nc.vector.tensor_scalar(y_all[:, bass.ds(g, 1)], pooled[:, :], inv_sum[:, 0:1], bp_col[:, 0:1],
                                        ALU.mult, ALU.add).then_inc(y_ready, 1)

            def body(v, last=False):
                for e in range(BODY):
                    if not (last and e >= BODY - 2):
                        residual(BODY * v + e + 2, (e + 2) % BODY)
                    if not last:
                        multiply(BODY * (v + 1) + e, e)

            multiply(0, 0)
            multiply(1, 1)
            dve.wait_ge(params, 16 * N_PARAMS)
            nc.vector.tensor_copy(w_high[:, :], w_block[:, :]).then_inc(w_high_ready, 1)
            dve.wait_ge(w_high_ready, 1)
            nc.vector.tensor_tensor(w_low[:, :], w_block[:, :], w_high[:, :].bitcast(fp32),
                                    ALU.subtract).then_inc(w_low_ready, 1)
            residual(0, 0)
            multiply(2, 2)
            residual(1, 1)
            multiply(3, 3)
            body(0)
            with dve.Fori(1, GROUP_BODIES) as v:
                body(v)
            pool_group(0)
            with dve.Fori(1, GROUPS - 1) as g:
                with dve.Fori(0, GROUP_BODIES) as w:
                    body(GROUP_BODIES * g + w)
                pool_group(g)
            with dve.Fori(BODIES - GROUP_BODIES, BODIES - 1) as v:
                body(v)
            body(BODIES - 1, last=True)
            pool_group(GROUPS - 1)

        @block.scalar
        def _(act):
            def spread(unit, slot):
                cols = x_cols[:, 0:UNIT_DUOS * FIELDS].rearrange("p (u f) -> p u f", f=FIELDS)
                act.wait_ge(x_transposed, unit + 1)
                if not (isinstance(unit, int) and unit < 2):
                    act.wait_ge(prod_ready, 2 * unit - 2)
                nc.scalar.copy(x_wide[:, slot, :, 0:FIELDS], cols).then_inc(x_spread, 1)
                nc.scalar.copy(x_wide[:, slot, :, FIELDS:WIDE], cols[:, :, 0:OFFSETS]).then_inc(x_spread, 1)

            def place_heads(w):
                first = head_cols[:, :, bass.ds(15 - (BODY - 1) - BODY * w, 32)]
                windows = bass.AP(first.tensor, first.offset, [first.ap[0], first.ap[1], [1, BODY], [1, 32]])
                nc.scalar.copy(head_w[:, :, :, :], windows).then_inc(head_w_ready, 1)

            def rectify(step, parity, q):
                if q == 0 and not (isinstance(step, int) and step < 2):
                    act.wait_ge(logits_done, step - 1)
                act.wait_ge(z_ready, QUADS * step + q + 1)
                nc.scalar.activation(hidden[:, parity, q, :].rearrange("p (b n) -> p b n", b=2),
                                     z[:, q % 2, :, 0:ZCOLS], ACT.Relu,
                                     bias=b_col[:, 0:1]).then_inc(hidden_ready, 1)

            def round_high(step, e, q):
                act.wait_ge(prod_ready, step + 1)
                nc.scalar.copy(high[:, e, q, :], prod[:, e, q, :]).then_inc(high_ready, 1)

            def exponentials(g):
                act.wait_ge(bias_ready, g + 1)
                nc.scalar.activation(exps[:, :, :], logits, ACT.Exp, bias=exp_bias[:, 0:1],
                                     accum_out=exp_sum[:, :]).then_inc(exps_ready, 1)

            def body(group, w, last=False):
                v = GROUP_BODIES * group + w
                for e in range(BODY):
                    step = BODY * v + e
                    for q in range(QUADS):
                        if not (last and e == BODY - 1):
                            rectify(step + 1, (e + 1) % 2, q)
                        if e == 0 and q == 0:
                            place_heads(w)
                        split = q - 1 if e == 0 else q
                        if 0 <= split < SPLIT and not (last and e > 0):
                            round_high(step + 3, (e + 3) % BODY, split)
                    if e == 0 and SPLIT == QUADS:
                        round_high(step + 3, (e + 3) % BODY, SPLIT - 1)
                    if e % 2 == 1 and not (isinstance(v, int) and 2 * v + 3 + e // 2 >= UNITS):
                        spread(2 * v + 3 + e // 2, (1 + e // 2) % 2)

            spread(0, 0)
            spread(1, 1)
            for step in range(2):
                for q in range(SPLIT):
                    round_high(step, step, q)
            spread(2, 0)
            act.wait_ge(params, 16 * N_PARAMS)
            for q in range(QUADS):
                rectify(0, 0, q)
                if q < SPLIT:
                    round_high(2, 2, q)
            body(0, 0)
            with act.Fori(1, GROUP_BODIES) as w:
                body(0, w)
            exponentials(0)
            with act.Fori(1, GROUPS - 1) as g:
                with act.Fori(0, GROUP_BODIES) as w:
                    body(g, w)
                exponentials(g)
            with act.Fori(0, GROUP_BODIES - 2) as w:
                body(GROUPS - 1, w)
            body(GROUPS - 1, GROUP_BODIES - 2)
            body(GROUPS - 1, GROUP_BODIES - 1, last=True)
            exponentials(GROUPS - 1)

        @block.tensor
        def _(pe):
            def transpose_unit(unit, slot, loads):
                pe.wait_ge(x_loaded[slot], 32 * loads)
                if not (isinstance(unit, int) and unit == 0):
                    pe.wait_ge(x_spread, 2 * unit)
                for c in range(CHUNKS):
                    last = nc.tensor.transpose(x_cols[:, c * ROWS:(c + 1) * ROWS], x_rows[:, slot, c, :], ident[:, :])
                last.then_inc(x_transposed, 1)

            def hidden_layer(step, e, q):
                if q == 0:
                    pe.wait_ge(low_ready, step + 1)
                if not (isinstance(step, int) and QUADS * step + q < 2):
                    pe.wait_ge(hidden_ready, QUADS * step + q - 1)
                for b in range(2):
                    cols = slice(b * ZCOLS, (b + 1) * ZCOLS)
                    if q < SPLIT:
                        passes = ((w_high, high[:, e, q, cols]), (w_high, low[:, e, q, cols]),
                                  (w_low, high[:, e, q, cols]))
                    else:
                        passes = ((w_block, prod[:, e, q, cols]),)
                    for n, (weights, moving) in enumerate(passes):
                        last = nc.tensor.matmul(z[:, q % 2, b, 0:ZCOLS], weights[:, :], moving,
                                                start=n == 0, stop=n == len(passes) - 1)
                last.then_inc(z_ready, 1)

            def open_group(g):
                if not (isinstance(g, int) and g == 0):
                    pe.wait_ge(pooled_ready, g)
                for b in range(3):
                    nc.tensor.matmul(heads[:, 2 * b:2 * b + 2, :], zero_row[:, 0:P], zero_row[:, :],
                                     start=True, stop=False, skip_group_check=True)

            def head(kind, source, e):
                for c in range(3):
                    for q in range(QUADS):
                        last = nc.tensor.matmul(heads[32 * q:32 * q + 32, 3 * kind + c, 0:HCOLS],
                                                head_w[:, kind, BODY - 1 - e, :],
                                                source[:, q, c * HCOLS:(c + 1) * HCOLS],
                                                start=False, stop=True, skip_group_check=True,
                                                tile_position=(0, 32 * q))
                return last

            def value_head(e):
                head(1, prod[:, e, :, :], e).then_inc(values_done, 1)

            def logit_head(step, e):
                pe.wait_ge(hidden_ready, QUADS * (step + 1))
                head(0, hidden[:, e % 2, :, :], e).then_inc(logits_done, 1)

            def body(v, opens=None, last=False):
                for e in range(BODY):
                    step = BODY * v + e
                    for q in range(QUADS):
                        if q == 2 and e > 0:
                            value_head(e)
                        if not (last and e == BODY - 1):
                            hidden_layer(step + 1, (e + 1) % BODY, q)
                    if e % 2 == 1:
                        unit = 2 * v + 3 + e // 2
                        if not (isinstance(v, int) and unit >= UNITS):
                            transpose_unit(unit, (1 + e // 2) % 2, v + 2 + e // 2)
                    if e == 0:
                        pe.wait_ge(head_w_ready, v + 1)
                        if opens is not None:
                            open_group(opens)
                        value_head(e)
                    logit_head(step, e)

            pe.wait_ge(ident_ready, 2)
            for unit in range(3):
                transpose_unit(unit, unit % 2, unit // 2 + 1)
            pe.wait_ge(params, 16 * N_PARAMS)
            pe.wait_ge(w_low_ready, 1)
            for q in range(QUADS):
                hidden_layer(0, 0, q)
            body(0, opens=0)
            with pe.Fori(1, GROUP_BODIES) as v:
                body(v)
            with pe.Fori(1, GROUPS - 1) as g:
                body(GROUP_BODIES * g, opens=g)
                with pe.Fori(1, GROUP_BODIES) as w:
                    body(GROUP_BODIES * g + w)
            body(BODIES - GROUP_BODIES, opens=GROUPS - 1)
            with pe.Fori(BODIES - GROUP_BODIES + 1, BODIES - 2) as v:
                body(v)
            body(BODIES - 2)
            body(BODIES - 1, last=True)


_INS = ['r_x', 'L0_rec_W_w', 'L0_rec_b_w', 'L0_rec_W_h', 'L0_rec_b_h', 'L0_rec_W_p', 'L0_rec_b_p']
_OUTS = [((2048, 1), 'float32')]


def kernel(**inputs):
    import numpy as _np
    import concourse.bacc as _bacc
    from concourse import mybir as _mybir
    from concourse.bass_utils import run_bass_kernel_spmd as _run

    nc = _bacc.Bacc("TRN2", target_bir_lowering=False, num_devices=1)
    arrays, args = {}, []
    for name in _INS:
        a = _np.ascontiguousarray(inputs[name])
        arrays[f"in_{name}_dram"] = a
        args.append(nc.dram_tensor(f"in_{name}_dram", a.shape, _mybir.dt.from_np(a.dtype), kind="ExternalInput").ap())
    for i, (shape, dtype) in enumerate(_OUTS):
        dt = _mybir.dt.from_np(_np.dtype(dtype))
        args.append(nc.dram_tensor(f"out_{i}_dram", shape, dt, kind="ExternalOutput").ap())
    bass_pairwise_attention_pooling(nc, *args)
    r = _run(nc, [arrays], core_ids=[0])
    return r.results[0]["out_0_dram"]
```

```python
import concourse.bass as bass
from concourse import mybir
from contextlib import ExitStack


def bass_pairwise_attention_pooling(
    nc: bass.Bass,
    x: bass.AP,
    w_hidden: bass.AP,
    b_hidden: bass.AP,
    w_logit: bass.AP,
    b_logit: bass.AP,
    w_out: bass.AP,
    b_out: bass.AP,
    y: bass.AP,
):
    fp32r = mybir.dt.float32r
    fp32 = mybir.dt.float32
    bf16 = mybir.dt.bfloat16
    ALU = mybir.AluOpType
    ACT = mybir.ActivationFunctionType
    AX = mybir.AxisListType

    BATCHES, FIELDS, D = x.shape
    A = w_hidden.shape[1]
    P = 2 * D
    assert P == 128 and A == D and FIELDS % 2 == 1
    HALF = BATCHES // 2
    OFFSETS = FIELDS // 2
    PAIRS = FIELDS * OFFSETS
    WIDE = FIELDS + OFFSETS

    QUADS = 4
    BODY = 4
    GROUP_STEPS = P // 2 // QUADS
    GROUP_BODIES = GROUP_STEPS // BODY
    GROUPS = HALF // (GROUP_STEPS * QUADS)
    BODIES = GROUPS * GROUP_BODIES

    UNIT_DUOS = 2 * QUADS
    UNITS = HALF // UNIT_DUOS
    CHUNKS = UNIT_DUOS // 2
    ROWS = 2 * FIELDS
    HALF_DUOS = UNIT_DUOS // 2

    BANK = 512
    PCOLS = PAIRS + 1
    ZCOLS = (PCOLS + 3) // 4 * 2
    ZPARTS = (slice(0, ZCOLS), slice(ZCOLS, PCOLS))
    HCOLS = (PAIRS + 1) // 2
    LOWEST = -3.0e38
    XCOLS = slice(ZCOLS, ZCOLS + ROWS)
    assert ZCOLS + ROWS <= BANK

    x_rows_dram = x.rearrange("(h c r) f d -> h (r f) c d", h=2, r=2)
    y_dram = y.rearrange("(h g t q) o -> q h t (g o)", h=2, g=GROUPS, q=QUADS)

    ctx = ExitStack()
    with ctx:
        def sb(name, shape, dt=fp32):
            return ctx.enter_context(nc.sbuf_tensor(name, shape, dt))

        def ps(name, shape):
            return ctx.enter_context(nc.psum_tensor(name, shape, fp32))

        def sem(name):
            return ctx.enter_context(nc.semaphore(name))

        w_block = sb("w_block", [P, P])
        w_high = sb("w_high", [P, P], fp32r)
        w_low = sb("w_low", [P, P], fp32r)
        b_col = sb("b_col", [P, 1])
        head_cols = sb("head_cols", [P, 2, 32 + GROUP_STEPS - 1])
        head_w = sb("head_w", [P, 2, BODY, 32])
        bh_col = sb("bh_col", [P, 1])
        bp_col = sb("bp_col", [P, 1])
        ident = sb("ident", [ROWS, ROWS])
        ones_row = sb("ones_row", [1, P], bf16)
        zero_row = sb("zero_row", [1, HCOLS], bf16)
        last_row = sb("last_row", [1, HCOLS], bf16)
        x_rows = sb("x_rows", [ROWS, 2, CHUNKS, 2 * D])
        x_wide = sb("x_wide", [P, 2, UNIT_DUOS, WIDE])
        prod = sb("prod", [P, BODY, QUADS, PCOLS])
        high = sb("high", [P, BODY, QUADS, PCOLS], fp32r)
        low = sb("low", [P, BODY, QUADS, PCOLS], fp32r)
        hidden = sb("hidden", [P, 2, QUADS, 2 * ZCOLS])
        neg_max = sb("neg_max", [P, 1])
        exp_bias = sb("exp_bias", [P, 1])
        exps = sb("exps", [P, 2, HCOLS])
        weighted = sb("weighted", [P, 2, HCOLS])
        exp_sum = sb("exp_sum", [P, 1])
        pooled = sb("pooled", [P, 1])
        inv_sum = sb("inv_sum", [P, 1])
        y_all = sb("y_all", [P, GROUPS])

        z = ps("z", [P, 2, 2, BANK])
        heads = ps("heads", [P, 2, 2, BANK])

        zeroed = sem("zeroed")
        params = sem("params")
        ident_ready = sem("ident_ready")
        x_loaded = [sem("x_loaded0"), sem("x_loaded1")]
        x_transposed = sem("x_transposed")
        x_spread = sem("x_spread")
        prod_ready = sem("prod_ready")
        w_high_ready = sem("w_high_ready")
        w_low_ready = sem("w_low_ready")
        high_ready = sem("high_ready")
        low_ready = sem("low_ready")
        z_ready = sem("z_ready")
        hidden_ready = sem("hidden_ready")
        head_w_ready = sem("head_w_ready")
        values_done = sem("values_done")
        logits_done = sem("logits_done")
        max_ready = sem("max_ready")
        bias_ready = sem("bias_ready")
        exps_ready = sem("exps_ready")
        pooled_ready = sem("pooled_ready")
        inv_ready = sem("inv_ready")
        y_ready = sem("y_ready")
        y_stored = sem("y_stored")

        N_PARAMS = 10

        block = ctx.enter_context(nc.Block())

        @block.sync
        def _(sp):
            def load(unit, slot):
                for h in range(2):
                    sp.dma_start(x_rows[:, slot, :, h * D:(h + 1) * D],
                                 x_rows_dram[h, :, bass.ds(unit * CHUNKS, CHUNKS), :]).then_inc(x_loaded[slot], 16)

            load(0, 0)
            load(1, 1)
            sp.wait_ge(zeroed, 1)
            for h in range(2):
                rows = slice(h * D, (h + 1) * D)
                at = GROUP_STEPS - 1 + GROUP_STEPS * h
                sp.dma_start(w_block[rows, rows], w_hidden).then_inc(params, 16)
                sp.dma_start(b_col[rows, :], b_hidden.rearrange("(a o) -> a o", o=1)).then_inc(params, 16)
                sp.dma_start(head_cols[rows, 0, at:at + 1],
                             w_logit.rearrange("(a o) -> a o", o=1)).then_inc(params, 16)
                sp.dma_start(head_cols[rows, 1, at:at + 1], w_out).then_inc(params, 16)
            for col, scalar in ((bh_col, b_logit), (bp_col, b_out)):
                sp.dma_start(col[:, :],
                             scalar.rearrange("(a o) -> a o", o=1).broadcast_to((P, 1))).then_inc(params, 16)

            with sp.Fori(1, UNITS // 2) as u:
                for slot in range(2):
                    sp.wait_ge(x_transposed, 2 * u + slot - 1)
                    load(2 * u + slot, slot)

            sp.wait_ge(y_ready, GROUPS)
            for q in range(QUADS):
                for h in range(2):
                    at = 32 * q + 16 * h
                    sp.dma_start(y_dram[q, h, :, :], y_all[at:at + GROUP_STEPS, :],
                                 allow_slow_non_contiguous=True).then_inc(y_stored, 16)
            sp.wait_ge(y_stored, 16 * 2 * QUADS)

        @block.gpsimd
        def _(pool):
            nc.gpsimd.memset(ident[:, :], 0.0).then_inc(ident_ready, 1)
            pool.wait_ge(ident_ready, 1)
            nc.gpsimd.affine_select(out=ident[:, :], in_=ident[:, :], compare_op=ALU.not_equal, fill=1.0,
                                    base=0, pattern=[[-1, ROWS]], channel_multiplier=1).then_inc(ident_ready, 1)

        @block.vector
        def _(dve):
            nc.vector.memset(w_block[:, :], 0.0)
            nc.vector.memset(ones_row[:, :], 1.0)
            nc.vector.memset(zero_row[:, :], 0.0)
            nc.vector.memset(last_row[:, 0:HCOLS - 1], 0.0)
            nc.vector.memset(last_row[:, HCOLS - 1:HCOLS], LOWEST)
            nc.vector.memset(prod[:, :, :, PAIRS:PCOLS], 0.0)
            nc.vector.memset(z[:, :, 1, PCOLS - ZCOLS:ZCOLS], 0.0)
            nc.vector.memset(head_cols[:, :, :], 0.0).then_inc(zeroed, 1)

            def multiply(step, e):
                slot, duo = e // 2, QUADS * (e % 2)
                x0 = x_wide[:, slot, duo:duo + QUADS, 0:FIELDS]
                one = bass.AP(x0.tensor, x0.offset, [x0.ap[0], x0.ap[1], [0, OFFSETS], x0.ap[2]])
                x1 = x_wide[:, slot, duo:duo + QUADS, 1:1 + FIELDS]
                other = bass.AP(x1.tensor, x1.offset, [x1.ap[0], x1.ap[1], [1, OFFSETS], x1.ap[2]])
                dve.wait_ge(x_spread, 2 * (step - e) + 4 * (e // 2) + 4)
                if not (isinstance(step, int) and step < BODY):
                    dve.wait_ge(values_done, step - BODY + 1)
                nc.vector.tensor_tensor(
                    prod[:, e, :, 0:PAIRS].rearrange("p q (k i) -> p q k i", k=OFFSETS), one, other,
                    ALU.mult).then_inc(prod_ready, 1)

            def residual(step, e):
                dve.wait_ge(high_ready, step + 1)
                nc.vector.tensor_tensor(low[:, e, :, :], prod[:, e, :, :], high[:, e, :, :].bitcast(fp32),
                                        ALU.subtract).then_inc(low_ready, 1)

            def pool_group(g):
                dve.wait_ge(values_done, GROUP_STEPS * (g + 1))
                dve.wait_ge(logits_done, GROUP_STEPS * (g + 1))
                nc.vector.tensor_reduce(neg_max[:, :], heads[:, 0, :, 0:HCOLS], AX.XY, ALU.max,
                                        negate=True).then_inc(max_ready, 1)
                dve.wait_ge(max_ready, g + 1)
                nc.vector.tensor_scalar(exp_bias[:, :], neg_max[:, :], bh_col[:, 0:1], bh_col[:, 0:1],
                                        ALU.subtract, ALU.add).then_inc(bias_ready, 1)
                dve.wait_ge(exps_ready, g + 1)
                nc.vector.tensor_tensor_reduce(out=weighted[:, :, :], in0=exps[:, :, :],
                                               in1=heads[:, 1, :, 0:HCOLS], scale=1.0, scalar=0.0,
                                               op0=ALU.mult, op1=ALU.add, accum_out=pooled[:, :]).then_inc(pooled_ready, 1)
                nc.vector.reciprocal(inv_sum[:, :], exp_sum[:, :]).then_inc(inv_ready, 1)
                dve.wait_ge(pooled_ready, g + 1)
                dve.wait_ge(inv_ready, g + 1)
                nc.vector.tensor_scalar(y_all[:, bass.ds(g, 1)], pooled[:, :], inv_sum[:, 0:1], bp_col[:, 0:1],
                                        ALU.mult, ALU.add).then_inc(y_ready, 1)

            def body(v, last=False):
                for e in range(BODY):
                    if not (last and e >= BODY - 2):
                        residual(BODY * v + e + 2, (e + 2) % BODY)
                    if not last:
                        multiply(BODY * (v + 1) + e, e)

            multiply(0, 0)
            multiply(1, 1)
            dve.wait_ge(params, 16 * N_PARAMS)
            nc.vector.tensor_copy(w_high[:, :], w_block[:, :]).then_inc(w_high_ready, 1)
            dve.wait_ge(w_high_ready, 1)
            nc.vector.tensor_tensor(w_low[:, :], w_block[:, :], w_high[:, :].bitcast(fp32),
                                    ALU.subtract).then_inc(w_low_ready, 1)
            residual(0, 0)
            multiply(2, 2)
            residual(1, 1)
            multiply(3, 3)
            body(0)
            with dve.Fori(1, GROUP_BODIES) as v:
                body(v)
            pool_group(0)
            with dve.Fori(1, GROUPS - 1) as g:
                with dve.Fori(0, GROUP_BODIES) as w:
                    body(GROUP_BODIES * g + w)
                pool_group(g)
            with dve.Fori(BODIES - GROUP_BODIES, BODIES - 1) as v:
                body(v)
            body(BODIES - 1, last=True)
            pool_group(GROUPS - 1)

        @block.scalar
        def _(act):
            def spread(unit, slot, half):
                x_cols = z[:, half, :, XCOLS].rearrange("p b (r f) -> p b r f", f=FIELDS)
                duos = slice(half * HALF_DUOS, (half + 1) * HALF_DUOS)
                wide = x_wide[:, slot, duos, :].rearrange("p (b r) f -> p b r f", b=2)
                if not (isinstance(unit, int) and unit < 2):
                    act.wait_ge(prod_ready, 2 * unit - 2)
                nc.scalar.copy(wide[:, :, :, 0:FIELDS], x_cols).then_inc(x_spread, 1)
                nc.scalar.copy(wide[:, :, :, FIELDS:WIDE], x_cols[:, :, :, 0:OFFSETS]).then_inc(x_spread, 1)

            def place_heads(w, half):
                first = head_cols[:, :, bass.ds(GROUP_STEPS - 1 - (BODY * w + 2 * half + 1), 32)]
                windows = bass.AP(first.tensor, first.offset, [first.ap[0], first.ap[1], [1, 2], [1, 32]])
                nc.scalar.copy(head_w[:, :, 2 - 2 * half:4 - 2 * half, :], windows).then_inc(head_w_ready, 1)

            def rectify(step, parity, q, unit=None, slot=None):
                if q == 0 and not (isinstance(step, int) and step < 2):
                    act.wait_ge(logits_done, step - 1)
                act.wait_ge(z_ready, QUADS * step + q + 1)
                if unit is not None:
                    spread(unit, slot, q % 2)
                nc.scalar.activation(hidden[:, parity, q, :].rearrange("p (b n) -> p b n", b=2),
                                     z[:, q % 2, :, 0:ZCOLS], ACT.Relu,
                                     bias=b_col[:, 0:1]).then_inc(hidden_ready, 1)

            def round_high(step, e):
                act.wait_ge(prod_ready, step + 1)
                nc.scalar.copy(high[:, e, :, :], prod[:, e, :, :]).then_inc(high_ready, 1)

            def exponentials(g):
                act.wait_ge(bias_ready, g + 1)
                nc.scalar.activation(exps[:, :, :], heads[:, 0, :, 0:HCOLS], ACT.Exp, bias=exp_bias[:, 0:1],
                                     accum_out=exp_sum[:, :]).then_inc(exps_ready, 1)

            def body(group, w, last=False, ended=None):
                v = GROUP_BODIES * group + w
                for e in range(BODY):
                    step = BODY * v + e
                    for q in range(QUADS):
                        unit, slot = None, None
                        if e % 2 == 1 and q >= 2 and not (isinstance(v, int) and 2 * v + 3 + e // 2 >= UNITS):
                            unit, slot = 2 * v + 3 + e // 2, (1 + e // 2) % 2
                        if not (last and e == BODY - 1):
                            rectify(step + 1, (e + 1) % 2, q, unit, slot)
                        if e == 0 and q == 0:
                            place_heads(w, 1)
                        if e == 2 and q == 0 and not last:
                            place_heads(0 if isinstance(w, int) and w == GROUP_BODIES - 1 else w + 1, 0)
                        if e == 0 and q == 0 and ended is not None:
                            exponentials(ended)
                        if q == 1 and not (last and e > 0):
                            round_high(step + 3, (e + 3) % BODY)

            for unit in range(2):
                act.wait_ge(x_transposed, unit + 1)
                for half in range(2):
                    spread(unit, unit % 2, half)
            round_high(0, 0)
            round_high(1, 1)
            act.wait_ge(x_transposed, 3)
            for half in range(2):
                spread(2, 0, half)
            act.wait_ge(params, 16 * N_PARAMS)
            place_heads(0, 0)
            for q in range(QUADS):
                rectify(0, 0, q)
                if q == 1:
                    round_high(2, 2)
            body(0, 0)
            with act.Fori(1, GROUP_BODIES - 1) as w:
                body(0, w)
            body(0, GROUP_BODIES - 1)
            with act.Fori(1, GROUPS - 1) as g:
                body(g, 0, ended=g - 1)
                with act.Fori(1, GROUP_BODIES - 1) as w:
                    body(g, w)
                body(g, GROUP_BODIES - 1)
            body(GROUPS - 1, 0, ended=GROUPS - 2)
            with act.Fori(1, GROUP_BODIES - 2) as w:
                body(GROUPS - 1, w)
            body(GROUPS - 1, GROUP_BODIES - 2)
            body(GROUPS - 1, GROUP_BODIES - 1, last=True)
            exponentials(GROUPS - 1)

        @block.tensor
        def _(pe):
            def transpose_half(slot, half):
                for b in range(2):
                    last = nc.tensor.transpose(z[:, half, b, XCOLS], x_rows[:, slot, 2 * half + b, :], ident[:, :])
                return last

            def hidden_layer(step, e, q, slot=None, loads=None):
                if q == 0:
                    pe.wait_ge(low_ready, step + 1)
                if not (isinstance(step, int) and QUADS * step + q < 2):
                    pe.wait_ge(hidden_ready, QUADS * step + q - 1)
                if slot is not None:
                    if q == 2:
                        pe.wait_ge(x_loaded[slot], 32 * loads)
                    transposed = transpose_half(slot, q % 2)
                    if q == 3:
                        transposed.then_inc(x_transposed, 1)
                passes = ((w_high, high), (w_high, low), (w_low, high))
                if q % 2 == 1:
                    passes = passes[::-1]
                for n, (weights, part) in enumerate(passes):
                    for b, cols in enumerate(ZPARTS):
                        last = nc.tensor.matmul(z[:, q % 2, b, 0:cols.stop - cols.start], weights[:, :],
                                                part[:, e, q, cols], start=n == 0, stop=n == len(passes) - 1)
                last.then_inc(z_ready, 1)

            def open_group(g):
                if not (isinstance(g, int) and g == 0):
                    pe.wait_ge(pooled_ready, g)
                for kind in range(2):
                    for b in range(2):
                        row = last_row if kind == 0 and b == 1 else zero_row
                        nc.tensor.matmul(heads[:, kind, b, 0:HCOLS], ones_row[:, :], row[:, :],
                                         start=True, stop=False, skip_group_check=True)

            def head(kind, source, e):
                for b in range(2):
                    cols = HCOLS - b
                    for q in range(QUADS):
                        last = nc.tensor.matmul(heads[32 * q:32 * q + 32, kind, b, 0:cols],
                                                head_w[:, kind, BODY - 1 - e, :],
                                                source[:, q, b * HCOLS:b * HCOLS + cols],
                                                start=False, stop=True, skip_group_check=True,
                                                tile_position=(0, 32 * q))
                return last

            def value_head(e):
                head(1, prod[:, e, :, :], e).then_inc(values_done, 1)

            def logit_head(step, e):
                pe.wait_ge(hidden_ready, QUADS * (step + 1))
                head(0, hidden[:, e % 2, :, :], e).then_inc(logits_done, 1)

            def body(v, opens=None, last=False):
                for e in range(BODY):
                    step = BODY * v + e
                    slot, loads = None, None
                    if e % 2 == 1 and not (isinstance(v, int) and 2 * v + 3 + e // 2 >= UNITS):
                        slot, loads = (1 + e // 2) % 2, v + 2 + e // 2
                    for q in range(QUADS):
                        if q == 2:
                            if e % 2 == 0:
                                pe.wait_ge(head_w_ready, 2 * v + 1 + e // 2)
                            if not (e == 0 and opens is not None):
                                value_head(e)
                        if not (last and e == BODY - 1):
                            hidden_layer(step + 1, (e + 1) % BODY, q, slot if q >= 2 else None, loads)
                    if e == 0 and opens is not None:
                        open_group(opens)
                        value_head(e)
                    logit_head(step, e)

            pe.wait_ge(ident_ready, 2)
            pe.wait_ge(zeroed, 1)
            for unit in range(3):
                pe.wait_ge(x_loaded[unit % 2], 32 * (unit // 2 + 1))
                if unit > 0:
                    pe.wait_ge(x_spread, 4 * unit)
                transpose_half(unit % 2, 0)
                transpose_half(unit % 2, 1).then_inc(x_transposed, 1)
            pe.wait_ge(x_spread, 12)
            pe.wait_ge(params, 16 * N_PARAMS)
            pe.wait_ge(w_low_ready, 1)
            for q in range(QUADS):
                hidden_layer(0, 0, q)
            body(0, opens=0)
            with pe.Fori(1, GROUP_BODIES) as v:
                body(v)
            with pe.Fori(1, GROUPS - 1) as g:
                body(GROUP_BODIES * g, opens=g)
                with pe.Fori(1, GROUP_BODIES) as w:
                    body(GROUP_BODIES * g + w)
            body(BODIES - GROUP_BODIES, opens=GROUPS - 1)
            with pe.Fori(BODIES - GROUP_BODIES + 1, BODIES - 2) as v:
                body(v)
            body(BODIES - 2)
            body(BODIES - 1, last=True)


_INS = ['r_x', 'L0_rec_W_w', 'L0_rec_b_w', 'L0_rec_W_h', 'L0_rec_b_h', 'L0_rec_W_p', 'L0_rec_b_p']
_OUTS = [((2048, 1), 'float32')]


def kernel(**inputs):
    import numpy as _np
    import concourse.bacc as _bacc
    from concourse import mybir as _mybir
    from concourse.bass_utils import run_bass_kernel_spmd as _run

    nc = _bacc.Bacc("TRN2", target_bir_lowering=False, num_devices=1)
    arrays, args = {}, []
    for name in _INS:
        a = _np.ascontiguousarray(inputs[name])
        arrays[f"in_{name}_dram"] = a
        args.append(nc.dram_tensor(f"in_{name}_dram", a.shape, _mybir.dt.from_np(a.dtype), kind="ExternalInput").ap())
    for i, (shape, dtype) in enumerate(_OUTS):
        dt = _mybir.dt.from_np(_np.dtype(dtype))
        args.append(nc.dram_tensor(f"out_{i}_dram", shape, dt, kind="ExternalOutput").ap())
    bass_pairwise_attention_pooling(nc, *args)
    r = _run(nc, [arrays], core_ids=[0])
    return r.results[0]["out_0_dram"]
```
